# Optimizing a Trainium2 kernel written in Bass

```python
import numpy as np
import jax
import jax.numpy as jnp

def _softmax(x, axis=-1):
    return jax.nn.softmax(x, axis=axis)
def _gelu(x):
    return jax.nn.gelu(x, approximate=True)
def _silu(x):
    return jax.nn.silu(x)
def _sigmoid(x):
    return jax.nn.sigmoid(x)
def _layernorm(x, axis=-1, eps=1e-5):
    m = jnp.mean(x, axis=axis, keepdims=True)
    v = jnp.var(x, axis=axis, keepdims=True)
    return (x - m) / jnp.sqrt(v + eps)
def _scatter_add(tgt, idx, src, axis=0):
    return tgt.at[idx].add(src)
def _segment_sum(src, seg, n):
    return jax.ops.segment_sum(src, seg, n)

kernel_name = 'mk_rec_standalone_d1_rec_9885f0'

def setup_inputs(seed: int = 0):
    np.random.seed(seed)
    _w = jnp.asarray
    def _rec_inputs():
        import jax
        import jax.numpy as jnp
        _rk = jax.random.key(seed)
        r_inputs = -8.4926e-05 + 0.999906 * jax.random.normal(jax.random.fold_in(_rk, 1), (4096, 201, 64), jnp.float32)
        return r_inputs
    r_inputs = _rec_inputs()
    def _L0_rec_setup():
        import jax, jax.numpy as jnp
        import numpy as np
        BN_EPS = 0.001
        NEG_SLOPE = 0.0003

        def _bn(x, gamma, beta, mean, var):
            return (x - mean) * jax.lax.rsqrt(var + BN_EPS) * gamma + beta
        key = jax.random.key(seed)
        ks = jax.random.split(key, 24)
        B, T, D = (4096, 200, 64)
        s = lambda fan_in: 1.0 / np.sqrt(fan_in)
        return {'inputs': jax.random.normal(ks[0], (B, T + 1, D), dtype=jnp.float32), 'att_bn_gamma': jax.random.uniform(ks[1], (3 * D,), dtype=jnp.float32, minval=0.5, maxval=1.5), 'att_bn_beta': jax.random.normal(ks[2], (3 * D,), dtype=jnp.float32) * 0.1, 'att_bn_mean': jax.random.normal(ks[3], (3 * D,), dtype=jnp.float32) * 0.1, 'att_bn_var': jax.random.uniform(ks[4], (3 * D,), dtype=jnp.float32, minval=0.5, maxval=1.5), 'att_W1': jax.random.normal(ks[5], (3 * D, 128), dtype=jnp.float32) * s(3 * D), 'att_b1': jnp.zeros((128,), jnp.float32), 'att_W2': jax.random.normal(ks[6], (128, 64), dtype=jnp.float32) * s(128), 'att_b2': jnp.zeros((64,), jnp.float32), 'att_W3': jax.random.normal(ks[7], (64, 1), dtype=jnp.float32) * s(64), 'att_b3': jnp.zeros((1,), jnp.float32), 'din_bn_gamma': jax.random.uniform(ks[8], (2 * D,), dtype=jnp.float32, minval=0.5, maxval=1.5), 'din_bn_beta': jax.random.normal(ks[9], (2 * D,), dtype=jnp.float32) * 0.1, 'din_bn_mean': jax.random.normal(ks[10], (2 * D,), dtype=jnp.float32) * 0.1, 'din_bn_var': jax.random.uniform(ks[11], (2 * D,), dtype=jnp.float32, minval=0.5, maxval=1.5), 'din_W1': jax.random.normal(ks[12], (2 * D, 200), dtype=jnp.float32) * s(2 * D), 'din_b1': jnp.zeros((200,), jnp.float32), 'din_W2': jax.random.normal(ks[13], (200, 80), dtype=jnp.float32) * s(200), 'din_b2': jnp.zeros((80,), jnp.float32), 'f_W': jax.random.normal(ks[14], (80, 1), dtype=jnp.float32) * s(80), 'f_b': jnp.zeros((1,), jnp.float32)}
    _L0_rec_all = _L0_rec_setup()
    _L0_rec_in = {k: v for k, v in _L0_rec_all.items() if k in ('att_bn_gamma', 'att_bn_beta', 'att_bn_mean', 'att_bn_var', 'att_W1', 'att_b1', 'att_W2', 'att_b2', 'att_W3', 'att_b3', 'din_bn_gamma', 'din_bn_beta', 'din_bn_mean', 'din_bn_var', 'din_W1', 'din_b1', 'din_W2', 'din_b2', 'f_W', 'f_b', )}
    del _L0_rec_all

    return {
        "r_inputs": r_inputs,
        "L0_rec_att_bn_gamma": _L0_rec_in["att_bn_gamma"],
        "L0_rec_att_bn_beta": _L0_rec_in["att_bn_beta"],
        "L0_rec_att_bn_mean": _L0_rec_in["att_bn_mean"],
        "L0_rec_att_bn_var": _L0_rec_in["att_bn_var"],
        "L0_rec_att_W1": _L0_rec_in["att_W1"],
        "L0_rec_att_b1": _L0_rec_in["att_b1"],
        "L0_rec_att_W2": _L0_rec_in["att_W2"],
        "L0_rec_att_b2": _L0_rec_in["att_b2"],
        "L0_rec_att_W3": _L0_rec_in["att_W3"],
        "L0_rec_att_b3": _L0_rec_in["att_b3"],
        "L0_rec_din_bn_gamma": _L0_rec_in["din_bn_gamma"],
        "L0_rec_din_bn_beta": _L0_rec_in["din_bn_beta"],
        "L0_rec_din_bn_mean": _L0_rec_in["din_bn_mean"],
        "L0_rec_din_bn_var": _L0_rec_in["din_bn_var"],
        "L0_rec_din_W1": _L0_rec_in["din_W1"],
        "L0_rec_din_b1": _L0_rec_in["din_b1"],
        "L0_rec_din_W2": _L0_rec_in["din_W2"],
        "L0_rec_din_b2": _L0_rec_in["din_b2"],
        "L0_rec_f_W": _L0_rec_in["f_W"],
        "L0_rec_f_b": _L0_rec_in["f_b"],
    }

def reference(r_inputs, L0_rec_att_bn_gamma, L0_rec_att_bn_beta, L0_rec_att_bn_mean, L0_rec_att_bn_var, L0_rec_att_W1, L0_rec_att_b1, L0_rec_att_W2, L0_rec_att_b2, L0_rec_att_W3, L0_rec_att_b3, L0_rec_din_bn_gamma, L0_rec_din_bn_beta, L0_rec_din_bn_mean, L0_rec_din_bn_var, L0_rec_din_W1, L0_rec_din_b1, L0_rec_din_W2, L0_rec_din_b2, L0_rec_f_W, L0_rec_f_b):
    import jax
    import jax.numpy as jnp
    def _L0_rec_ref(inputs, att_bn_gamma, att_bn_beta, att_bn_mean, att_bn_var, att_W1, att_b1, att_W2, att_b2, att_W3, att_b3, din_bn_gamma, din_bn_beta, din_bn_mean, din_bn_var, din_W1, din_b1, din_W2, din_b2, f_W, f_b):
        import jax, jax.numpy as jnp
        import numpy as np
        BN_EPS = 0.001
        NEG_SLOPE = 0.0003

        def _bn(x, gamma, beta, mean, var):
            return (x - mean) * jax.lax.rsqrt(var + BN_EPS) * gamma + beta
        user_click = inputs[:, :-1, :]
        news = inputs[:, -1, :]
        sub = news[:, None, :] - user_click
        news_b = jnp.broadcast_to(news[:, None, :], user_click.shape)
        emb = jnp.concatenate([user_click, sub, news_b], axis=-1)
        h = _bn(emb, att_bn_gamma, att_bn_beta, att_bn_mean, att_bn_var)
        h = jax.nn.relu(jnp.einsum('btf,fh->bth', h, att_W1) + att_b1)
        h = jax.nn.relu(jnp.einsum('bth,hk->btk', h, att_W2) + att_b2)
        ai = jax.nn.sigmoid(jnp.einsum('btk,ko->bto', h, att_W3) + att_b3)
        user = jnp.sum(ai * user_click, axis=1)
        x = jnp.concatenate([user, news], axis=-1)
        x = _bn(x, din_bn_gamma, din_bn_beta, din_bn_mean, din_bn_var)
        x = x @ din_W1 + din_b1
        x = jnp.where(x > 0, x, NEG_SLOPE * x)
        x = x @ din_W2 + din_b2
        x = jnp.where(x > 0, x, NEG_SLOPE * x)
        y = jax.nn.sigmoid(x @ f_W + f_b)
        return y

    y = _L0_rec_ref(r_inputs, L0_rec_att_bn_gamma, L0_rec_att_bn_beta, L0_rec_att_bn_mean, L0_rec_att_bn_var, L0_rec_att_W1, L0_rec_att_b1, L0_rec_att_W2, L0_rec_att_b2, L0_rec_att_W3, L0_rec_att_b3, L0_rec_din_bn_gamma, L0_rec_din_bn_beta, L0_rec_din_bn_mean, L0_rec_din_bn_var, L0_rec_din_W1, L0_rec_din_b1, L0_rec_din_W2, L0_rec_din_b2, L0_rec_f_W, L0_rec_f_b)
    return y


_drawn_inputs = setup_inputs


def setup_inputs(seed=0):
    import zlib

    import numpy as np

    out = dict(_drawn_inputs(seed))
    spreads = {'L0_rec_att_b1': (0.0, 0.582),
     'L0_rec_att_b2': (0.0, 0.524),
     'L0_rec_din_b1': (0.0, 0.505),
     'L0_rec_din_b2': (0.0, 0.576)}
    factors = {'L0_rec_att_bn_beta': 3.948,
     'L0_rec_att_bn_mean': 2.919,
     'L0_rec_din_bn_beta': 4.758,
     'L0_rec_din_bn_mean': 3.979}
    for name, (base, spread) in spreads.items():
        noise = np.random.default_rng([zlib.crc32(name.encode()), seed]).standard_normal(out[name].shape)
        drawn = base * np.exp(spread * noise) if base else spread * noise
        out[name] = jnp.asarray(drawn.astype(out[name].dtype))
    for name, factor in factors.items():
        out[name] = (out[name] * factor).astype(out[name].dtype)
    return out
```

```python
from contextlib import ExitStack

import concourse.bass as bass
from concourse import mybir

ALU = mybir.AluOpType
ACT = mybir.ActivationFunctionType
AX = mybir.AxisListType
F32 = mybir.dt.float32
F32R = mybir.dt.float32r

BN_EPS = 0.001
NEG_SLOPE = 0.0003


def attention_head(
    nc: bass.Bass,
    r_inputs: bass.AP,
    att_gamma: bass.AP, att_beta: bass.AP, att_mean: bass.AP, att_var: bass.AP,
    att_W1: bass.AP, att_b1: bass.AP, att_W2: bass.AP, att_b2: bass.AP, att_W3: bass.AP, att_b3: bass.AP,
    din_gamma: bass.AP, din_beta: bass.AP, din_mean: bass.AP, din_var: bass.AP,
    din_W1: bass.AP, din_b1: bass.AP, din_W2: bass.AP, din_b2: bass.AP,
    f_W: bass.AP, f_b: bass.AP,
    out: bass.AP,
):
    B, T1, D = r_inputs.shape
    T = T1 - 1
    F1 = att_W1.shape[1]
    F2 = att_W2.shape[1]
    P = 128
    BLOCKS = B // P
    CT = 8
    HALF = CT // 2
    GC = 5
    GT = GC * CT
    GROUPS = T // GT
    CHUNKS = BLOCKS * GROUPS * GC
    CW = CT * D
    CC = CT * P
    HC = HALF * P
    BANK = 512
    ZT = GC * HALF // 4
    ZC = ZT * P
    ND1, ND2 = din_W1.shape[1], din_W2.shape[1]
    NH = ND1 // 2
    NB = B // BANK
    BPB = BANK // P
    assert (D, F1, F2, P * BLOCKS, GT * GROUPS) == (64, 128, 64, B, T) and GROUPS == GC == 5

    with ExitStack() as ctx:
        def sb(name, shape, dt=F32):
            return ctx.enter_context(nc.sbuf_tensor(name, shape, dt))

        def psum(name, shape):
            return ctx.enter_context(nc.psum_tensor(name, shape, F32))

        def sem(name):
            return ctx.enter_context(nc.semaphore(name))

        ps_turn = psum("ps_turn", [P, CC])
        ps_x = psum("ps_x", [P, CC])
        ps_y = psum("ps_y", [P, BANK])
        ps_z = psum("ps_z", [P, 2 * BANK])
        ps_m = psum("ps_m", [P, BANK])

        u = sb("u", [P, GROUPS, GC * CW])
        split = sb("split", [P, GC, CT, 2 * D], F32R)
        xT = sb("xT", [P, GC, CC], F32R)
        h1 = sb("h1", [P, GC, CC])
        h2 = sb("h2", [P, GC * HC])
        zS = sb("zS", [P, ZC])
        att = sb("att", [P, GROUPS, GT])
        prod = sb("prod", [P, GC, CW])
        part = sb("part", [P, GROUPS * GC, D])
        user = sb("user", [P, BLOCKS, D])
        catT = sb("catT", [P, B])
        neg_c = sb("neg_c", [P, B])
        neg_g = sb("neg_g", [P, B])
        z0 = sb("z0", [P, BLOCKS])
        news = h1[:, 0:3, :].rearrange("p a b -> p (a b)")[:, 0:(BLOCKS + 1) * D].rearrange("p (s d) -> p s d", d=D)

        ident = sb("ident", [P, P])
        ident_r = sb("ident_r", [P, P], F32R)
        w1a, w1b, w1c = (sb(f"w1{x}", [P, F1]) for x in "abc")
        w1bs = sb("w1bs", [P, F1])
        wu = sb("wu", [P, F1])
        wu_h = sb("wu_h", [P, F1], F32R)
        wu_l = sb("wu_l", [P, F1], F32R)
        wn = sb("wn", [P, F1])
        w2 = sb("w2", [P, F2])
        w3 = sb("w3", [P, 1])
        w3_rep = sb("w3_rep", [P, 32])
        b1c, b2c, b3c, c0 = (sb(n, [P, 1]) for n in ("b1c", "b2c", "b3c", "c0"))
        bn = sb("bn", [P, 4, 4])
        bn_v, bn_q, bn_r, bn_t, bn_s, bn_b = (sb(f"bn_{x}", [P, 4]) for x in "vqrtsb")
        wd1 = sb("wd1", [P, ND1])
        wd1s = sb("wd1s", [P, ND1])
        wd2 = sb("wd2", [NH, 2, ND2])
        fw = sb("fw", [ND2, 1])
        bd1, bd1s = sb("bd1", [NH, 2]), sb("bd1s", [NH, 2])
        bd2 = sb("bd2", [ND2, 1])
        fb = sb("fb", [1, 1])
        score = u[0:1, :, :].rearrange("p a n -> p (a n)")[:, 0:B]

        split_h_done = sem("split_h_done")
        split_done = sem("split_done")
        turn_done = sem("turn_done")
        xT_done = sem("xT_done")
        x_done = sem("x_done")
        h1_done = sem("h1_done")
        y_done = sem("y_done")
        h2_done = sem("h2_done")
        prod_done = sem("prod_done")
        part_done = sem("part_done")
        u_loaded = sem("u_loaded")
        z_done = sem("z_done")
        zS_done = sem("zS_done")
        zT_done = sem("zT_done")
        att_done = sem("att_done")
        user_done = sem("user_done")
        params_loaded = sem("params_loaded")
        news_loaded = sem("news_loaded")
        ident_set = sem("ident_set")
        dve_step = sem("dve_step")
        root_done = sem("root_done")
        bias_mm = sem("bias_mm")
        weights_ready = sem("weights_ready")
        pre_mm = sem("pre_mm")
        pre_out = sem("pre_out")
        negated = sem("negated")
        userT_mm = sem("userT_mm")
        userT_out = sem("userT_out")
        d1_mm, d1_sum, d1_act = sem("d1_mm"), sem("d1_sum"), sem("d1_act")
        d2_mm, d2_sum, d2_act = sem("d2_mm"), sem("d2_sum"), sem("d2_act")
        d3_mm, d3_out = sem("d3_mm"), sem("d3_out")
        stored = sem("stored")

        r_blocks = r_inputs.rearrange("(s p) t d -> s p (t d)", p=P)

        def wait(eng, sem_, n):
            if not isinstance(n, int) or n > 0:
                eng.wait_ge(sem_, n)

        def exists(k):
            return not isinstance(k, int) or 0 <= k < CHUNKS

        def back(s, g, n):
            if isinstance(g, int):
                return (s, g - n) if g >= n else (s - 1, g - n + GROUPS)
            return s, g - n

        def all_groups(eng, group):
            group(-1, GROUPS - 1)
            group(0, 0)
            group(0, 1)
            group(0, 2)
            with eng.Fori(3, GROUPS) as g:
                group(0, g)
            with eng.Fori(1, BLOCKS - 1) as s:
                group(s, 0)
                group(s, 1)
                with eng.Fori(2, GROUPS) as g:
                    group(s, g)
            group(BLOCKS - 1, 0)
            group(BLOCKS - 1, 1)
            with eng.Fori(2, GROUPS - 1) as g:
                group(BLOCKS - 1, g)
            group(BLOCKS - 1, GROUPS - 1)
            group(BLOCKS, 0)
            group(BLOCKS, 1)

        def clicks(s, g, c):
            return u[:, bass.ds(g, 1), c * CW:(c + 1) * CW].rearrange("p a (q h d) -> p h (a q) d", h=2, d=D)

        def ahead(s, g):
            if isinstance(g, int):
                return (s, g + 1) if g + 1 < GROUPS else (s + 1, 0)
            return s, (g + 1) % GROUPS

        def half_view(c, part_):
            return split[:, c, :, part_ * D:(part_ + 1) * D].rearrange("p (h q) d -> p h q d", h=2)

        PARAMS = 2 * 9 + 4 + 9

        def d1p(b, h):
            return (ps_turn, ps_x)[b % 2][0:NH, h * BANK:(h + 1) * BANK]

        def d2p(b):
            return (ps_y, ps_m)[b % 2][0:ND2, :]

        def d3p(b):
            return ps_z[0:1, (b % 2) * BANK:(b % 2 + 1) * BANK]

        def d1s(b, h):
            return neg_c[0:NH, (2 * (b % 2) + h) * BANK:(2 * (b % 2) + h + 1) * BANK]

        def d1v(b, h):
            return neg_c[0:NH, (4 + 2 * (b % 2) + h) * BANK:(4 + 2 * (b % 2) + h + 1) * BANK]

        def d2s(b):
            return neg_g[0:ND2, (b % 2) * BANK:(b % 2 + 1) * BANK]

        def d2v(b):
            return neg_g[0:ND2, (2 + b % 2) * BANK:(3 + b % 2) * BANK]

        block = ctx.enter_context(nc.Block())

        @block.sync
        def _(sp):
            sp.dma_start(news[:, 1:, :], r_inputs[:, T, :].rearrange("(s p) d -> p s d", p=P)).then_inc(news_loaded, 16)
            sp.dma_start(news[:, 0, :], r_inputs[0:P, T, :]).then_inc(news_loaded, 16)

            def load(s, g, first):
                G = s * GROUPS + g
                src = r_blocks[bass.ds(s, 1), :, bass.ds(g * (GT * D), GT * D)].rearrange("a p n -> (a p) n")
                wait(sp, u_loaded, G * 16)
                if not first:
                    sp.wait_ge(prod_done, (G - GROUPS + 1) * GC)
                sp.dma_start(u[:, bass.ds(g, 1), :].rearrange("p a n -> p (a n)"), src).then_inc(u_loaded, 16)

            for g in range(GROUPS):
                load(0, g, True)
            with sp.Fori(1, BLOCKS) as s:
                with sp.Fori(0, GROUPS) as g:
                    load(s, g, False)
            sp.wait_ge(d3_out, NB)
            sp.dma_start(out.rearrange("b o -> o b"), score[:]).then_inc(stored, 16)
            sp.wait_ge(stored, 16)

        @block.gpsimd
        def _(pool):
            pool.memset(ident[:], 0.0).then_inc(ident_set, 1)
            pool.wait_ge(ident_set, 1)
            nc.gpsimd.affine_select(out=ident[:], in_=ident[:], compare_op=ALU.not_equal, fill=1.0, base=0,
                                    pattern=[[-1, P]], channel_multiplier=1).then_inc(ident_set, 1)

            def group(s, g):
                for c in range(GC):
                    k = (s * GROUPS + g) * GC + c
                    if exists(k + 3):
                        c3 = (c + 3) % GC
                        s3, g3 = (s, g) if c3 == c + 3 else ahead(s, g)
                        pool.wait_ge(split_h_done, k + 4)
                        nc.gpsimd.tensor_tensor(half_view(c3, 1), clicks(s3, g3, c3),
                                                half_view(c3, 0).bitcast(F32), ALU.subtract
                                                ).then_inc(split_done, 1)
                    if exists(k - 9):
                        cb = (c - 9) % GC
                        sb_, gb = back(s, g, (9 - c + GC - 1) // GC)
                        pool.wait_ge(att_done, sb_ * GROUPS + gb + 1)
                        wait(pool, part_done, k - 9 - GC + 1)
                        nc.gpsimd.tensor_tensor(
                            prod[:, cb, :].rearrange("p (t d) -> p t d", d=D),
                            u[:, bass.ds(gb, 1), cb * CW:(cb + 1) * CW].rearrange("p a (t d) -> p (a t) d", d=D),
                            att[:, bass.ds(gb, 1), cb * CT:(cb + 1) * CT].rearrange("p a t -> p (a t)")
                            .unsqueeze(2).to_broadcast([P, CT, D]),
                            ALU.mult).then_inc(prod_done, 1)

            all_groups(pool, group)

        @block.scalar
        def _(act):
            n = [0]

            def load(dst, src):
                act.dma_start(dst, src, allow_slow_non_contiguous=True).then_inc(params_loaded, 16)
                n[0] += 1

            for lo in (0, D):
                for j, w in enumerate((w1a, w1b, w1c)):
                    load(w[lo:lo + D, :], att_W1[j * D:(j + 1) * D, :])
                for i, v in enumerate((att_gamma, att_beta, att_mean, att_var)):
                    load(bn[lo:lo + D, i, 0:3], v.rearrange("(j p) -> p j", p=D))
                load(b2c[lo:lo + D, :], att_b2.rearrange("(p a) -> p a", a=1))
                load(w3[lo:lo + D, :], att_W3)
            for i, v in enumerate((din_gamma, din_beta, din_mean, din_var)):
                load(bn[:, i, 3:4], v.rearrange("(p a) -> p a", a=1))
            load(b1c[:], att_b1.rearrange("(p a) -> p a", a=1))
            load(b3c[:], att_b3.rearrange("(p a) -> p a", a=1).to_broadcast([P, 1]))
            load(w2[:], att_W2)
            load(wd1[:], din_W1)
            load(wd2[:], din_W2.rearrange("(h p) n -> p h n", p=NH))
            load(bd1[:], din_b1.rearrange("(h p) -> p h", p=NH))
            load(bd2[:], din_b2.rearrange("(p a) -> p a", a=1))
            load(fw[:], f_W)
            load(fb[:], f_b.rearrange("(p a) -> p a", a=1))
            assert n[0] == PARAMS

            act.wait_ge(dve_step, 1)
            act.activation(bn_q[:], bn_v[:], ACT.Sqrt).then_inc(root_done, 1)

            def take(step, dst, func=ACT.Copy, **kw):
                act.wait_ge(pre_mm, step + 1)
                act.activation(dst, ps_x[:, (step % 2) * BANK:(step % 2 + 1) * BANK], func, **kw).then_inc(pre_out, 1)

            for b in range(NB):
                take(b, catT[:, b * BANK:(b + 1) * BANK])
            act.wait_ge(weights_ready, 1)
            for b in range(NB):
                take(NB + b, neg_c[:, b * BANK:(b + 1) * BANK], ACT.Identity, bias=c0[:])
            for b in range(NB):
                take(2 * NB + b, neg_g[:, b * BANK:(b + 1) * BANK], ACT.Identity, bias=b2c[:])
            act.wait_ge(pre_mm, 3 * NB + 1)
            act.activation(h2[:, 0:2 * BANK], ps_z[:], ACT.Copy).then_inc(pre_out, 1)
            act.wait_ge(pre_mm, 3 * NB + 2)
            act.activation(z0[:].rearrange("p (r j v) -> p r v j", r=2, v=4),
                           ps_x[:].rearrange("p (r v j m) -> p r v j m", r=2, v=4, m=32)[:, :, :, :, 0],
                           ACT.Identity, bias=b3c[:]).then_inc(pre_out, 1)
            act.wait_ge(pre_out, 3 * NB + 2)

            def group(s, g):
                G = s * GROUPS + g
                for c in range(GC):
                    k = G * GC + c
                    if exists(k + 1):
                        act.wait_ge(turn_done, k + 2)
                        wait(act, x_done, k + 1 - GC + 1)
                        act.activation(xT[:, (c + 1) % GC, :], ps_turn[:], ACT.Copy).then_inc(xT_done, 1)
                    if c == 1 and exists(k - GC - 1):
                        wait(act, z_done, G)
                        act.activation(zS[:], ps_z[:, 0:ZC], ACT.Copy).then_inc(zS_done, 1)
                    if exists(k + 3):
                        c3 = (c + 3) % GC
                        s3, g3 = (s, g) if c3 == c + 3 else ahead(s, g)
                        if c3 == 0:
                            act.wait_ge(u_loaded, (G + 2) * 16)
                        wait(act, turn_done, k + 3 - GC + 1)
                        act.activation(half_view(c3, 0), clicks(s3, g3, c3), ACT.Copy).then_inc(split_h_done, 1)
                    if c == 2 and exists(k - GC - 1):
                        sa, ga = back(s, g, 1)
                        wait(act, zT_done, G)
                        if not (isinstance(s, int) and s == 0):
                            wait(act, prod_done, (G - GROUPS) * GC + 1)
                        act.activation(
                            att[:, bass.ds(ga, 1), :].rearrange("p a (j v h) -> p v (a j) h", j=4, h=2),
                            ps_z[:, 0:ZC].rearrange("p (v j h m) -> p v j h m", v=ZT, j=4, h=2)[:, :, :, :, 0],
                            ACT.Sigmoid, bias=z0[:, bass.ds(sa, 1)]).then_inc(att_done, 1)

            all_groups(act, group)

            for b in range(NB):
                act.wait_ge(userT_mm, b + 1)
                act.activation(catT[0:D, b * BANK:(b + 1) * BANK], ps_x[0:D, (b % 2) * BANK:(b % 2 + 1) * BANK],
                               ACT.Copy).then_inc(userT_out, 1)
            for step in range(NB + 2):
                if step < NB:
                    b = step
                    act.wait_ge(d1_mm, b + 1)
                    wait(act, d1_act, b - 1)
                    for h in range(2):
                        act.activation(d1s(b, h), d1p(b, h), ACT.Identity, bias=bd1s[:, h:h + 1]).then_inc(d1_sum, 1)
                if 1 <= step <= NB:
                    b = step - 1
                    act.wait_ge(d2_mm, b + 1)
                    wait(act, d2_act, b - 1)
                    act.activation(d2s(b), d2p(b), ACT.Identity, bias=bd2[:]).then_inc(d2_sum, 1)
                if step >= 2:
                    b = step - 2
                    act.wait_ge(d3_mm, b + 1)
                    act.activation(score[:, b * BANK:(b + 1) * BANK], d3p(b), ACT.Sigmoid, bias=fb[:]).then_inc(d3_out, 1)

        @block.tensor
        def _(pe):
            pe.wait_ge(dve_step, 8)
            for j, w in enumerate((w1a, w1b, w1c)):
                pe.matmul(ps_m[:, 0:1], w[D:P, :], bn_b[D:P, j:j + 1], start=(j == 0), stop=(j == 2))
            for h in range(2):
                mm = pe.matmul(ps_m[0:NH, 1 + h:2 + h], wd1[:, h * NH:(h + 1) * NH], bn_b[:, 3:4],
                               start=True, stop=True)
            mm.then_inc(bias_mm, 1)

            def target(step):
                wait(pe, pre_out, step - 1)
                return ps_x[:, (step % 2) * BANK:(step % 2 + 1) * BANK]

            pe.wait_ge(news_loaded, 32)
            pe.wait_ge(ident_set, 2)
            for b in range(NB):
                dst = target(b)
                for i in range(BPB):
                    s = b * BPB + i
                    mm = pe.transpose(dst[:, i * P:(i + 1) * P], news[:, s:s + 2, :].rearrange("p a d -> p (a d)"), ident[:])
                mm.then_inc(pre_mm, 1)
            pe.wait_ge(weights_ready, 1)
            for b in range(NB):
                dst = target(NB + b)
                pe.matmul(dst, wn[:], catT[:, b * BANK:(b + 1) * BANK], start=True, stop=True).then_inc(pre_mm, 1)
            for b in range(NB):
                dst = target(2 * NB + b)
                pe.wait_ge(pre_out, NB + b + 1)
                for h in range(2):
                    mm = pe.matmul(dst[h * F2:(h + 1) * F2, :], w2[:], neg_c[:, b * BANK:(b + 1) * BANK],
                                   start=True, stop=True)
                mm.then_inc(pre_mm, 1)
            pe.wait_ge(pre_out, 3 * NB)
            for b in range(NB):
                mm = pe.matmul(ps_z[32 * (b % 4):32 * (b % 4) + 32, (b // 4) * BANK:(b // 4 + 1) * BANK], w3_rep[:],
                               neg_g[:, b * BANK:(b + 1) * BANK], start=True, stop=True)
            mm.then_inc(pre_mm, 1)
            pe.wait_ge(pre_out, 3 * NB + 1)
            for v in range(NB):
                mm = pe.transpose(ps_x[:, v * P:(v + 1) * P], h2[:, v * P:(v + 1) * P], ident[:])
            mm.then_inc(pre_mm, 1)

            def group(s, g):
                G = s * GROUPS + g
                for c in range(GC):
                    k = G * GC + c
                    c1 = (c + 1) % GC
                    if exists(k + 1):
                        pe.wait_ge(split_done, k + 2)
                        wait(pe, xT_done, k + 1)
                        for i in range(CT):
                            mm = pe.transpose(ps_turn[:, i * P:(i + 1) * P].bitcast(F32R), split[:, c1, i, :], ident_r[:])
                        mm.then_inc(turn_done, 1)
                    if exists(k):
                        pe.wait_ge(xT_done, k + 1)
                        if isinstance(k, int) and k == 0:
                            pe.wait_ge(pre_out, 3 * NB + 2)
                        wait(pe, h1_done, k)
                        for h in range(2):
                            half = xT[:, c, h * HC:(h + 1) * HC]
                            pe.matmul(ps_x[:, h * HC:(h + 1) * HC], wu_h[:], half, start=True, stop=False)
                            mm = pe.matmul(ps_x[:, h * HC:(h + 1) * HC], wu_l[:], half, start=False, stop=True)
                        mm.then_inc(x_done, 1)
                    if c == 1 and exists(k - GC - 1):
                        wait(pe, h2_done, G * GC)
                        wait(pe, att_done, G - 1)
                        for lo, hi in ((0, BANK), (BANK, ZC)):
                            for j in range(4):
                                mm = pe.matmul(ps_z[32 * j:32 * j + 32, lo:hi], w3_rep[:], h2[:, j * ZC + lo:j * ZC + hi],
                                               start=True, stop=True)
                        mm.then_inc(z_done, 1)
                    if c == 2 and exists(k - GC - 1):
                        wait(pe, zS_done, G)
                        for v in range(ZT):
                            mm = pe.transpose(ps_z[:, v * P:(v + 1) * P], zS[:, v * P:(v + 1) * P], ident[:])
                        mm.then_inc(zT_done, 1)
                    if exists(k - 1):
                        cb = (c - 1) % GC
                        wait(pe, h1_done, k)
                        wait(pe, h2_done, k - 1)
                        for h in range(2):
                            mm = pe.matmul(ps_y[h * F2:(h + 1) * F2, :], w2[:], h1[:, cb, h * HC:(h + 1) * HC],
                                           start=True, stop=True)
                        mm.then_inc(y_done, 1)

            all_groups(pe, group)

            pe.wait_ge(user_done, BLOCKS)
            for b in range(NB):
                wait(pe, userT_out, b - 1)
                for i in range(BPB):
                    mm = pe.transpose(ps_x[0:D, (b % 2) * BANK + i * P:(b % 2) * BANK + (i + 1) * P],
                                      user[:, b * BPB + i, :], ident[:])
                mm.then_inc(userT_mm, 1)
            pe.wait_ge(userT_out, NB)
            for step in range(NB + 2):
                if step < NB:
                    b = step
                    wait(pe, d1_sum, 2 * (b - 1))
                    for h in range(2):
                        mm = pe.matmul(d1p(b, h), wd1s[:, h * NH:(h + 1) * NH], catT[:, b * BANK:(b + 1) * BANK],
                                       start=True, stop=True)
                    mm.then_inc(d1_mm, 1)
                if 1 <= step <= NB:
                    b = step - 1
                    pe.wait_ge(d1_act, b + 1)
                    wait(pe, d2_sum, b - 1)
                    for h in range(2):
                        mm = pe.matmul(d2p(b), wd2[:, h, :], d1v(b, h), start=(h == 0), stop=(h == 1))
                    mm.then_inc(d2_mm, 1)
                if step >= 2:
                    b = step - 2
                    pe.wait_ge(d2_act, b + 1)
                    wait(pe, d3_out, b - 1)
                    pe.matmul(d3p(b), fw[:], d2v(b), start=True, stop=True).then_inc(d3_mm, 1)

        @block.vector
        def _(dve):
            steps = [0]

            def link(ins):
                steps[0] += 1
                ins.then_inc(dve_step, 1)
                dve.wait_ge(dve_step, steps[0])

            dve.wait_ge(params_loaded, 16 * PARAMS)
            link(dve.tensor_scalar(bn_v[:], bn[:, 3, :], BN_EPS, None, ALU.add))
            dve.wait_ge(root_done, 1)
            link(dve.reciprocal(bn_r[:], bn_q[:]))
            link(dve.tensor_tensor(bn_t[:], bn_r[:], bn_r[:], ALU.mult))
            link(dve.scalar_tensor_tensor(bn_q[:], bn_t[:], -0.5, bn_v[:], ALU.mult, ALU.mult))
            link(dve.scalar_tensor_tensor(bn_t[:], bn_q[:], 1.5, bn_r[:], ALU.add, ALU.mult))
            link(dve.tensor_tensor(bn_s[:], bn[:, 0, :], bn_t[:], ALU.mult))
            link(dve.tensor_tensor(bn_r[:], bn[:, 2, :], bn_s[:], ALU.mult))
            link(dve.tensor_tensor(bn_b[:], bn[:, 1, :], bn_r[:], ALU.subtract))
            link(dve.tensor_scalar(w1bs[:], w1b[:], bn_s[:, 1:2], None, ALU.mult))
            link(dve.scalar_tensor_tensor(wu[:], w1a[:], bn_s[:, 0:1], w1bs[:], ALU.mult, ALU.subtract))
            link(dve.tensor_copy(wu_h[:], wu[:]))
            link(dve.tensor_tensor(wu_l[:], wu[:], wu_h[:].bitcast(F32), ALU.subtract))
            link(dve.memset(wn[0:D, :], 0.0))
            link(dve.scalar_tensor_tensor(wn[D:P, :], w1c[D:P, :], bn_s[D:P, 2:3], w1bs[D:P, :], ALU.mult, ALU.add))
            link(dve.memset(w3_rep[:], 0.0))
            for h in range(2):
                link(dve.tensor_copy(w3_rep[h * F2:(h + 1) * F2, 16 * h:16 * h + 16],
                                     w3[h * F2:(h + 1) * F2, :].to_broadcast([F2, 16])))
            link(dve.tensor_scalar(wd1s[:], wd1[:], bn_s[:, 3:4], None, ALU.mult))
            dve.wait_ge(ident_set, 2)
            link(dve.tensor_copy(ident_r[:], ident[:]))
            dve.wait_ge(bias_mm, 1)
            link(dve.tensor_tensor(c0[:], ps_m[:, 0:1], b1c[:], ALU.add))
            dve.tensor_tensor(bd1s[:], ps_m[0:NH, 1:3], bd1[:], ALU.add).then_inc(weights_ready, 1)
            dve.wait_ge(pre_mm, 3 * NB)
            dve.tensor_scalar(neg_c[:], neg_c[:], -1.0, None, ALU.mult).then_inc(negated, 1)
            dve.wait_ge(pre_mm, 3 * NB + 1)
            dve.tensor_scalar(neg_g[:], neg_g[:], -1.0, None, ALU.mult).then_inc(negated, 1)
            dve.wait_ge(negated, 2)

            def group(s, g):
                G = s * GROUPS + g
                for c in range(GC):
                    k = G * GC + c
                    if exists(k):
                        dve.wait_ge(x_done, k + 1)
                        wait(dve, y_done, k - GC + 1)
                        dve.tensor_tensor(h1[:, c, :].rearrange("p (t b) -> p t b", b=P),
                                          ps_x[:].rearrange("p (t b) -> p t b", b=P),
                                          neg_c[:, bass.ds(s * P, P)].unsqueeze(1).to_broadcast([P, CT, P]),
                                          ALU.max).then_inc(h1_done, 1)
                    if exists(k - 1):
                        cb = (c - 1) % GC
                        s2, g2 = (s, g) if c >= 1 else back(s, g, 1)
                        dve.wait_ge(y_done, k)
                        if cb == 0:
                            wait(dve, z_done, G)
                        dve.tensor_tensor(h2[:, cb * HC:(cb + 1) * HC].rearrange("p (t b) -> p t b", b=P),
                                          ps_y[:].rearrange("p (t b) -> p t b", b=P),
                                          neg_g[:, bass.ds(s2 * P, P)].unsqueeze(1).to_broadcast([P, HALF, P]),
                                          ALU.max).then_inc(h2_done, 1)
                    if exists(k - 10):
                        cb = (c - 10) % GC
                        sr, gr = back(s, g, 2)
                        dve.wait_ge(prod_done, k - 9)
                        if cb == 0 and not isinstance(g, int):
                            wait(dve, user_done, sr)
                        dve.tensor_reduce(part[:, bass.ds(gr * GC + cb, 1), :].rearrange("p a d -> p (a d)"),
                                          prod[:, cb, :].rearrange("p (t d) -> p d t", d=D),
                                          AX.X, ALU.add).then_inc(part_done, 1)
                    if c == GC - 1 and isinstance(g, int) and g == 1 and exists(k - 10):
                        if not (isinstance(s, int) and s == 0):
                            dve.wait_ge(part_done, k - 9)
                            dve.tensor_reduce(user[:, bass.ds(s - 1, 1), :].rearrange("p a d -> p (a d)"),
                                              part[:].rearrange("p r d -> p d r"), AX.X, ALU.add).then_inc(user_done, 1)

            all_groups(dve, group)

            for step in range(NB + 1):
                if step < NB:
                    b = step
                    dve.wait_ge(d1_sum, 2 * (b + 1))
                    wait(dve, d2_mm, b - 1)
                    dve.scalar_tensor_tensor(d1v(b, 0), d1s(b, 0), NEG_SLOPE, d1s(b, 0), ALU.mult, ALU.max)
                    dve.scalar_tensor_tensor(d1v(b, 1), d1s(b, 1), NEG_SLOPE, d1s(b, 1), ALU.mult, ALU.max
                                             ).then_inc(d1_act, 1)
                if step >= 1:
                    b = step - 1
                    dve.wait_ge(d2_sum, b + 1)
                    wait(dve, d3_mm, b - 1)
                    dve.scalar_tensor_tensor(d2v(b), d2s(b), NEG_SLOPE, d2s(b), ALU.mult, ALU.max).then_inc(d2_act, 1)


_INS = ["r_inputs"] + ["L0_rec_" + n for n in (
    "att_bn_gamma", "att_bn_beta", "att_bn_mean", "att_bn_var",
    "att_W1", "att_b1", "att_W2", "att_b2", "att_W3", "att_b3",
    "din_bn_gamma", "din_bn_beta", "din_bn_mean", "din_bn_var",
    "din_W1", "din_b1", "din_W2", "din_b2", "f_W", "f_b")]


def kernel(**inputs):
    import numpy as _np
    import concourse.bacc as _bacc
    from concourse import mybir as _mybir
    from concourse.bass_utils import run_bass_kernel_spmd as _run

    nc = _bacc.Bacc("TRN2", target_bir_lowering=False, num_devices=1)
    arrays, args = {}, []
    for name in _INS:
        a = _np.ascontiguousarray(inputs[name])
        arrays[f"in_{name}"] = a
        args.append(nc.dram_tensor(f"in_{name}", a.shape, _mybir.dt.from_np(a.dtype), kind="ExternalInput").ap())
    users = inputs["r_inputs"].shape[0]
    args.append(nc.dram_tensor("out_0", (users, 1), _mybir.dt.float32, kind="ExternalOutput").ap())
    attention_head(nc, *args)
    r = _run(nc, [arrays], core_ids=[0])
    return r.results[0]["out_0"]
```

```python
from contextlib import ExitStack

import concourse.bass as bass
from concourse import mybir

ALU = mybir.AluOpType
ACT = mybir.ActivationFunctionType
AX = mybir.AxisListType
F32 = mybir.dt.float32
F32R = mybir.dt.float32r

BN_EPS = 0.001
NEG_SLOPE = 0.0003


def attention_head(
    nc: bass.Bass,
    r_inputs: bass.AP,
    att_gamma: bass.AP, att_beta: bass.AP, att_mean: bass.AP, att_var: bass.AP,
    att_W1: bass.AP, att_b1: bass.AP, att_W2: bass.AP, att_b2: bass.AP, att_W3: bass.AP, att_b3: bass.AP,
    din_gamma: bass.AP, din_beta: bass.AP, din_mean: bass.AP, din_var: bass.AP,
    din_W1: bass.AP, din_b1: bass.AP, din_W2: bass.AP, din_b2: bass.AP,
    f_W: bass.AP, f_b: bass.AP,
    out: bass.AP,
):
    B, T1, D = r_inputs.shape
    T = T1 - 1
    F1 = att_W1.shape[1]
    F2 = att_W2.shape[1]
    P = 128
    BLOCKS = B // P
    CT = 8
    HALF = CT // 2
    GC = 5
    GT = GC * CT
    GROUPS = T // GT
    CHUNKS = BLOCKS * GROUPS * GC
    CW = CT * D
    CC = CT * P
    HC = HALF * P
    BANK = 512
    ND1, ND2 = din_W1.shape[1], din_W2.shape[1]
    NH = ND1 // 2
    NB = B // BANK
    BPB = BANK // P
    assert (D, F1, F2, P * BLOCKS, GT * GROUPS) == (64, 128, 64, B, T) and GROUPS == GC == 5

    with ExitStack() as ctx:
        def sb(name, shape, dt=F32):
            return ctx.enter_context(nc.sbuf_tensor(name, shape, dt))

        def psum(name, shape):
            return ctx.enter_context(nc.psum_tensor(name, shape, F32))

        def sem(name):
            return ctx.enter_context(nc.semaphore(name))

        ps_turn = psum("ps_turn", [P, CC])
        ps_x = psum("ps_x", [P, CC])
        ps_y = psum("ps_y", [P, 2 * BANK])
        ps_z = psum("ps_z", [P, BANK])
        ps_m = psum("ps_m", [P, BANK])

        u = sb("u", [P, GROUPS, GC * CW])
        split = sb("split", [P, GC, CT, 2 * D], F32R)
        xT = sb("xT", [P, GC, CC], F32R)
        h1 = sb("h1", [P, GC, CC])
        h2 = sb("h2", [P, GC * HC])
        zS = sb("zS", [P, P])
        att = sb("att", [P, GROUPS, GT])
        prod = sb("prod", [P, GC, CW + D])
        user = sb("user", [P, BLOCKS, D])
        catT = sb("catT", [P, B])
        neg_c = sb("neg_c", [P, B])
        neg_g = sb("neg_g", [P, B])
        z0 = sb("z0", [P, BLOCKS])
        news = h1[:, 0:3, :].rearrange("p a b -> p (a b)")[:, 0:(BLOCKS + 1) * D].rearrange("p (s d) -> p s d", d=D)

        ident = sb("ident", [P, P])
        ident_r = sb("ident_r", [P, P], F32R)
        w1 = sb("w1", [P, 3, F1])
        w1a, w1b, w1c = (w1[:, j, :] for j in range(3))
        w1bs = sb("w1bs", [P, F1])
        wu = sb("wu", [P, F1])
        wu_h = sb("wu_h", [P, F1], F32R)
        wu_l = sb("wu_l", [P, F1], F32R)
        wn = sb("wn", [P, F1])
        w2 = sb("w2", [P, F2])
        w3 = sb("w3", [P, 1])
        w3_at = sb("w3_at", [P, GC, 32])
        b1c, b2c, b3c, c0 = (sb(n, [P, 1]) for n in ("b1c", "b2c", "b3c", "c0"))
        bn = sb("bn", [P, 4, 4])
        bn_v, bn_q, bn_r, bn_t, bn_s, bn_b = (sb(f"bn_{x}", [P, 4]) for x in "vqrtsb")
        wd1 = sb("wd1", [P, ND1])
        wd1s = sb("wd1s", [P, ND1])
        wd2 = sb("wd2", [NH, 2, ND2])
        fw = sb("fw", [ND2, 1])
        bd1, bd1s = sb("bd1", [NH, 2]), sb("bd1s", [NH, 2])
        bd2 = sb("bd2", [ND2, 1])
        fb = sb("fb", [P, 1])
        fw_col = sb("fw_col", [ND2, 32])
        score = u[:, 0, 0:B // 4]

        split_h_done = sem("split_h_done")
        split_done = sem("split_done")
        turn_done = sem("turn_done")
        xT_done = sem("xT_done")
        x_done = sem("x_done")
        h1_done = sem("h1_done")
        y_done = sem("y_done")
        h2_done = sem("h2_done")
        prod_done = sem("prod_done")
        part_done = sem("part_done")
        z_done = sem("z_done")
        u_loaded = sem("u_loaded")
        zS_done = sem("zS_done")
        zT_done = sem("zT_done")
        att_done = sem("att_done")
        params_loaded = sem("params_loaded")
        params2_loaded = sem("params2_loaded")
        news_loaded = sem("news_loaded")
        ident_set = sem("ident_set")
        dve_step = sem("dve_step")
        root_done = sem("root_done")
        bias_mm = sem("bias_mm")
        weights_ready = sem("weights_ready")
        pre_mm = sem("pre_mm")
        pre_out = sem("pre_out")
        negated = sem("negated")
        userT_mm = sem("userT_mm")
        userT_out = sem("userT_out")
        d1_mm, d1_sum, d1_act = sem("d1_mm"), sem("d1_sum"), sem("d1_act")
        d2_mm, d2_sum, d2_act = sem("d2_mm"), sem("d2_sum"), sem("d2_act")
        d3_mm, d3_out = sem("d3_mm"), sem("d3_out")
        stored = sem("stored")

        r_blocks = r_inputs.rearrange("(s p) t d -> s p (t d)", p=P)

        def wait(eng, sem_, n):
            if not isinstance(n, int) or n > 0:
                eng.wait_ge(sem_, n)

        def exists(k):
            return not isinstance(k, int) or 0 <= k < CHUNKS

        def back(s, g, n):
            if isinstance(g, int):
                return (s, g - n) if g >= n else (s - 1, g - n + GROUPS)
            return s, g - n

        def all_groups(eng, group):
            group(-1, GROUPS - 1)
            group(0, 0)
            group(0, 1)
            group(0, 2)
            with eng.Fori(3, GROUPS) as g:
                group(0, g)
            with eng.Fori(1, BLOCKS - 1) as s:
                group(s, 0)
                group(s, 1)
                with eng.Fori(2, GROUPS) as g:
                    group(s, g)
            group(BLOCKS - 1, 0)
            group(BLOCKS - 1, 1)
            with eng.Fori(2, GROUPS - 1) as g:
                group(BLOCKS - 1, g)
            group(BLOCKS - 1, GROUPS - 1)
            group(BLOCKS, 0)
            group(BLOCKS, 1)

        def clicks(s, g, c):
            return u[:, bass.ds(g, 1), c * CW:(c + 1) * CW].rearrange("p a (q h d) -> p h (a q) d", h=2, d=D)

        def ahead(s, g):
            if isinstance(g, int):
                return (s, g + 1) if g + 1 < GROUPS else (s + 1, 0)
            return s, (g + 1) % GROUPS

        def half_view(c, part_):
            return split[:, c, :, part_ * D:(part_ + 1) * D].rearrange("p (h q) d -> p h q d", h=2)

        PARAMS, PARAMS2 = 2 * 7 + 3, 4 + 6
        DIN_SHIFT = 8 + 4 + 2 * GC + 4 + 8

        def y_bank(c):
            return ps_y[:, (c % 2) * BANK:(c % 2 + 1) * BANK]

        def d1p(b, h):
            return (ps_turn, ps_x)[b % 2][0:NH, h * BANK:(h + 1) * BANK]

        def d2p(b):
            return ps_y[0:ND2, (b % 2) * BANK:(b % 2 + 1) * BANK]

        def d1s(b, h):
            return neg_c[0:NH, (2 * (b % 2) + h) * BANK:(2 * (b % 2) + h + 1) * BANK]

        def d1v(b, h):
            return neg_c[0:NH, (4 + 2 * (b % 2) + h) * BANK:(4 + 2 * (b % 2) + h + 1) * BANK]

        def d2s(b):
            return h1[0:ND2, 0, (b % 2) * BANK:(b % 2 + 1) * BANK]

        def d2v(b):
            return neg_g[0:ND2, b * BANK:(b + 1) * BANK]

        block = ctx.enter_context(nc.Block())

        @block.sync
        def _(sp):
            sp.dma_start(news[:, 1:, :], r_inputs[:, T, :].rearrange("(s p) d -> p s d", p=P)).then_inc(news_loaded, 16)
            sp.dma_start(news[:, 0, :], r_inputs[0:P, T, :]).then_inc(news_loaded, 16)

            def load(s, g, first):
                G = s * GROUPS + g
                src = r_blocks[bass.ds(s, 1), :, bass.ds(g * (GT * D), GT * D)].rearrange("a p n -> (a p) n")
                wait(sp, u_loaded, G * 16)
                if not first:
                    sp.wait_ge(prod_done, (G - GROUPS + 1) * GC)
                sp.dma_start(u[:, bass.ds(g, 1), :].rearrange("p a n -> p (a n)"), src).then_inc(u_loaded, 16)

            for g in range(GROUPS):
                load(0, g, True)
            with sp.Fori(1, BLOCKS) as s:
                with sp.Fori(0, GROUPS) as g:
                    load(s, g, False)
            sp.wait_ge(d3_out, NB // 4)
            out_rows = out.rearrange("(r j n) o -> j r (n o)", j=4, n=BANK)
            for j in range(4):
                sp.dma_start(out_rows[j:j + 1], score[32 * j:32 * j + 1, :].rearrange("p (r n) -> p r n", n=BANK)
                             ).then_inc(stored, 16)
            sp.wait_ge(stored, 64)

        @block.gpsimd
        def _(pool):
            def load(dst, src):
                pool.dma_start(dst, src, allow_slow_non_contiguous=True).then_inc(params2_loaded, 16)

            for i, v in enumerate((din_gamma, din_beta, din_mean, din_var)):
                load(bn[:, i, 3:4], v.rearrange("(p a) -> p a", a=1))
            load(wd1[:], din_W1)
            load(wd2[:], din_W2.rearrange("(h p) n -> p h n", p=NH))
            load(bd1[:], din_b1.rearrange("(h p) -> p h", p=NH))
            load(bd2[:], din_b2.rearrange("(p a) -> p a", a=1))
            load(fw[:], f_W)
            load(fb[:], f_b.rearrange("(p a) -> p a", a=1).to_broadcast([P, 1]))

            pool.memset(ident[:], 0.0).then_inc(ident_set, 1)
            pool.wait_ge(ident_set, 1)
            nc.gpsimd.affine_select(out=ident[:], in_=ident[:], compare_op=ALU.not_equal, fill=1.0, base=0,
                                    pattern=[[-1, P]], channel_multiplier=1).then_inc(ident_set, 1)

            def group(s, g):
                for c in range(GC):
                    k = (s * GROUPS + g) * GC + c
                    if exists(k + 3):
                        c3 = (c + 3) % GC
                        s3, g3 = (s, g) if c3 == c + 3 else ahead(s, g)
                        pool.wait_ge(split_h_done, k + 4)
                        nc.gpsimd.tensor_tensor(half_view(c3, 1), clicks(s3, g3, c3),
                                                half_view(c3, 0).bitcast(F32), ALU.subtract
                                                ).then_inc(split_done, 1)
                    if exists(k - 9):
                        cb = (c - 9) % GC
                        sb_, gb = back(s, g, (9 - c + GC - 1) // GC)
                        pool.wait_ge(att_done, sb_ * GROUPS + gb + 1)
                        wait(pool, part_done, k - 9 - GC + 1)
                        nc.gpsimd.tensor_tensor(
                            prod[:, cb, 0:CW].rearrange("p (t d) -> p t d", d=D),
                            u[:, bass.ds(gb, 1), cb * CW:(cb + 1) * CW].rearrange("p a (t d) -> p (a t) d", d=D),
                            att[:, bass.ds(gb, 1), cb * CT:(cb + 1) * CT].rearrange("p a t -> p (a t)")
                            .unsqueeze(2).to_broadcast([P, CT, D]),
                            ALU.mult).then_inc(prod_done, 1)

            all_groups(pool, group)

        @block.scalar
        def _(act):
            def load(dst, src):
                act.dma_start(dst, src, allow_slow_non_contiguous=True).then_inc(params_loaded, 16)

            for lo in (0, D):
                for i, v in ((3, att_var), (0, att_gamma), (2, att_mean), (1, att_beta)):
                    load(bn[lo:lo + D, i, 0:3], v.rearrange("(j p) -> p j", p=D))
                load(w1[lo:lo + D, :, :], att_W1.rearrange("(j p) f -> p j f", p=D))
                load(b2c[lo:lo + D, :], att_b2.rearrange("(p a) -> p a", a=1))
                load(w3[lo:lo + D, :], att_W3)
            load(b1c[:], att_b1.rearrange("(p a) -> p a", a=1))
            load(b3c[:], att_b3.rearrange("(p a) -> p a", a=1).to_broadcast([P, 1]))
            load(w2[:], att_W2)

            act.wait_ge(dve_step, 1)
            act.activation(bn_q[:, 0:3], bn_v[:, 0:3], ACT.Sqrt).then_inc(root_done, 1)

            def take(step, dst, func=ACT.Copy, **kw):
                act.wait_ge(pre_mm, step + 1)
                act.activation(dst, ps_x[:, (step % 2) * BANK:(step % 2 + 1) * BANK], func, **kw).then_inc(pre_out, 1)

            for b in range(NB):
                take(b, catT[:, b * BANK:(b + 1) * BANK])
            act.wait_ge(weights_ready, 1)
            for b in range(NB):
                take(NB + b, neg_c[:, b * BANK:(b + 1) * BANK], ACT.Identity, bias=c0[:])
            act.wait_ge(dve_step, DIN_SHIFT - 7)
            act.activation(bn_q[:, 3:4], bn_v[:, 3:4], ACT.Sqrt).then_inc(root_done, 1)
            for b in range(NB):
                take(2 * NB + b, neg_g[:, b * BANK:(b + 1) * BANK], ACT.Identity, bias=b2c[:])
            act.wait_ge(pre_mm, 3 * NB + 1)
            act.activation(h2[:, 0:2 * BANK], ps_y[:], ACT.Copy).then_inc(pre_out, 1)
            act.wait_ge(pre_mm, 3 * NB + 2)
            act.activation(z0[:].rearrange("p (r j v) -> p r v j", r=2, v=4),
                           ps_x[:].rearrange("p (r v j m) -> p r v j m", r=2, v=4, m=32)[:, :, :, :, 0],
                           ACT.Identity, bias=b3c[:]).then_inc(pre_out, 1)
            act.wait_ge(pre_out, 3 * NB + 2)

            def group(s, g):
                G = s * GROUPS + g
                for c in range(GC):
                    k = G * GC + c
                    if exists(k + 1):
                        act.wait_ge(turn_done, k + 2)
                        wait(act, x_done, 2 * (k + 1 - GC + 1))
                        act.activation(xT[:, (c + 1) % GC, :], ps_turn[:], ACT.Copy).then_inc(xT_done, 1)
                    if exists(k + 3):
                        c3 = (c + 3) % GC
                        s3, g3 = (s, g) if c3 == c + 3 else ahead(s, g)
                        if c3 == 0:
                            act.wait_ge(u_loaded, (G + 2) * 16)
                        wait(act, turn_done, k + 3 - GC + 1)
                        act.activation(half_view(c3, 0), clicks(s3, g3, c3), ACT.Copy).then_inc(split_h_done, 1)
                    if c == 1 and exists(k - GC - 1):
                        wait(act, z_done, G * GC)
                        act.activation(zS[:], ps_z[:, 0:P], ACT.Copy).then_inc(zS_done, 1)
                    if c == 2 and exists(k - GC - 1):
                        sa, ga = back(s, g, 1)
                        wait(act, zT_done, G)
                        if not (isinstance(s, int) and s == 0):
                            wait(act, prod_done, (G - GROUPS) * GC + 1)
                        act.activation(
                            att[:, bass.ds(ga, 1), :].rearrange("p a (c q h) -> p (a c) q h", q=HALF, h=2),
                            ps_m[:, 0:P].rearrange("p (q m) -> p q m", m=32)[:, :, 0:2 * GC]
                            .rearrange("p q (c h) -> p c q h", h=2),
                            ACT.Sigmoid, bias=z0[:, bass.ds(sa, 1)]).then_inc(att_done, 1)

            all_groups(act, group)

            for step in range(-1, NB + 1):
                if step + 1 < NB:
                    b = step + 1
                    act.wait_ge(userT_mm, b + 1)
                    act.activation(catT[0:D, b * BANK:(b + 1) * BANK], ps_m[0:D, :], ACT.Copy).then_inc(userT_out, 1)
                if 0 <= step < NB:
                    b = step
                    act.wait_ge(d1_mm, b + 1)
                    wait(act, d1_act, b - 1)
                    for h in range(2):
                        act.activation(d1s(b, h), d1p(b, h), ACT.Identity, bias=bd1s[:, h:h + 1]).then_inc(d1_sum, 1)
                if step >= 1:
                    b = step - 1
                    act.wait_ge(d2_mm, b + 1)
                    wait(act, d2_act, b - 1)
                    act.activation(d2s(b), d2p(b), ACT.Identity, bias=bd2[:]).then_inc(d2_sum, 1)
            for r in range(NB // 4):
                act.wait_ge(d3_mm, r + 1)
                act.activation(score[:, r * BANK:(r + 1) * BANK], ps_z[:], ACT.Sigmoid, bias=fb[:]).then_inc(d3_out, 1)

        @block.tensor
        def _(pe):
            def target(step):
                wait(pe, pre_out, step - 1)
                return ps_x[:, (step % 2) * BANK:(step % 2 + 1) * BANK]

            pe.wait_ge(news_loaded, 32)
            pe.wait_ge(ident_set, 2)
            for b in range(NB):
                dst = target(b)
                for i in range(BPB):
                    s = b * BPB + i
                    mm = pe.transpose(dst[:, i * P:(i + 1) * P], news[:, s:s + 2, :].rearrange("p a d -> p (a d)"), ident[:])
                mm.then_inc(pre_mm, 1)
            pe.wait_ge(dve_step, 8)
            for j, w in enumerate((w1a, w1b, w1c)):
                mm = pe.matmul(ps_m[:, 0:1], w[D:P, :], bn_b[D:P, j:j + 1], start=(j == 0), stop=(j == 2))
            mm.then_inc(bias_mm, 1)
            pe.wait_ge(weights_ready, 1)
            for b in range(NB):
                dst = target(NB + b)
                pe.matmul(dst, wn[:], catT[:, b * BANK:(b + 1) * BANK], start=True, stop=True).then_inc(pre_mm, 1)
            for b in range(NB):
                dst = target(2 * NB + b)
                pe.wait_ge(pre_out, NB + b + 1)
                for h in range(2):
                    mm = pe.matmul(dst[h * F2:(h + 1) * F2, :], w2[:], neg_c[:, b * BANK:(b + 1) * BANK],
                                   start=True, stop=True)
                mm.then_inc(pre_mm, 1)
            pe.wait_ge(dve_step, DIN_SHIFT)
            for h in range(2):
                mm = pe.matmul(ps_m[0:NH, 1 + h:2 + h], wd1[:, h * NH:(h + 1) * NH], bn_b[:, 3:4],
                               start=True, stop=True)
            mm.then_inc(bias_mm, 1)
            pe.wait_ge(pre_out, 3 * NB)
            for b in range(NB):
                mm = pe.matmul(ps_y[32 * (b % 4):32 * (b % 4) + 32, (b // 4) * BANK:(b // 4 + 1) * BANK], w3_at[:, 0, :],
                               neg_g[:, b * BANK:(b + 1) * BANK], start=True, stop=True)
            mm.then_inc(pre_mm, 1)
            pe.wait_ge(pre_out, 3 * NB + 1)
            for v in range(NB):
                mm = pe.transpose(ps_x[:, v * P:(v + 1) * P], h2[:, v * P:(v + 1) * P], ident[:])
            mm.then_inc(pre_mm, 1)

            def group(s, g):
                G = s * GROUPS + g
                for c in range(GC):
                    k = G * GC + c
                    c1 = (c + 1) % GC
                    if exists(k + 1):
                        pe.wait_ge(split_done, k + 2)
                        wait(pe, xT_done, k + 1)
                        for i in range(CT):
                            mm = pe.transpose(ps_turn[:, i * P:(i + 1) * P].bitcast(F32R), split[:, c1, i, :], ident_r[:])
                        mm.then_inc(turn_done, 1)
                    if exists(k):
                        if isinstance(k, int) and k == CHUNKS - 1:
                            pe.wait_ge(xT_done, CHUNKS)
                        if isinstance(k, int) and k == 0:
                            pe.wait_ge(pre_out, 3 * NB + 2)
                        for h in range(2):
                            wait(pe, h1_done, 2 * (k - 1) + h + 1)
                            half = xT[:, c, h * HC:(h + 1) * HC]
                            pe.matmul(ps_x[:, h * HC:(h + 1) * HC], wu_h[:], half, start=True, stop=False)
                            pe.matmul(ps_x[:, h * HC:(h + 1) * HC], wu_l[:], half, start=False, stop=True
                                      ).then_inc(x_done, 1)
                    if c == 2 and exists(k - GC - 1):
                        wait(pe, zS_done, G)
                        wait(pe, att_done, G - 1)
                        pe.transpose(ps_m[:, 0:P], zS[:], ident[:]).then_inc(zT_done, 1)
                    if exists(k - 1):
                        cb = (c - 1) % GC
                        if isinstance(k, int) and k == CHUNKS:
                            pe.wait_ge(h1_done, 2 * CHUNKS)
                        if cb == 0:
                            wait(pe, h2_done, k - 1)
                        for h in range(2):
                            mm = pe.matmul(y_bank(cb)[h * F2:(h + 1) * F2, :], w2[:], h1[:, cb, h * HC:(h + 1) * HC],
                                           start=True, stop=True)
                        mm.then_inc(y_done, 1)
                    if exists(k - 2):
                        cb = (c - 2) % GC
                        wait(pe, h2_done, k - 1)
                        if cb == 0:
                            wait(pe, zS_done, G)
                        for q in range(HALF):
                            mm = pe.matmul(ps_z[32 * q:32 * q + 32, 0:P], w3_at[:, cb, :],
                                           h2[:, cb * HC + q * P:cb * HC + (q + 1) * P],
                                           start=(cb == 0), stop=(cb == GC - 1))
                        mm.then_inc(z_done, 1)

            all_groups(pe, group)

            for step in range(-1, NB + 2):
                if step + 1 < NB:
                    b = step + 1
                    pe.wait_ge(part_done, (b + 1) * BPB * GROUPS * GC)
                    wait(pe, userT_out, b)
                    if b == 0:
                        pe.wait_ge(att_done, CHUNKS // GC)
                    for i in range(BPB):
                        mm = pe.transpose(ps_m[0:D, i * P:(i + 1) * P], user[:, b * BPB + i, :], ident[:])
                    mm.then_inc(userT_mm, 1)
                if 0 <= step < NB:
                    b = step
                    pe.wait_ge(userT_out, b + 1)
                    wait(pe, d1_sum, 2 * (b - 1))
                    for h in range(2):
                        mm = pe.matmul(d1p(b, h), wd1s[:, h * NH:(h + 1) * NH], catT[:, b * BANK:(b + 1) * BANK],
                                       start=True, stop=True)
                    mm.then_inc(d1_mm, 1)
                if 1 <= step <= NB:
                    b = step - 1
                    pe.wait_ge(d1_act, b + 1)
                    wait(pe, d2_sum, b - 1)
                    for h in range(2):
                        mm = pe.matmul(d2p(b), wd2[:, h, :], d1v(b, h), start=(h == 0), stop=(h == 1))
                    mm.then_inc(d2_mm, 1)
                if step >= 5 and step % 4 == 1:
                    r = step // 4 - 1
                    pe.wait_ge(d2_act, 4 * r + 4)
                    wait(pe, d3_out, r)
                    for j in range(4):
                        mm = pe.matmul(ps_z[32 * j:32 * j + 32, :], fw_col[:], d2v(4 * r + j), start=True, stop=True)
                    mm.then_inc(d3_mm, 1)

        @block.vector
        def _(dve):
            steps = [0]

            def link(ins):
                steps[0] += 1
                ins.then_inc(dve_step, 1)
                dve.wait_ge(dve_step, steps[0])

            def batch_norms(cols):
                link(dve.tensor_scalar(bn_v[:, cols], bn[:, 3, cols], BN_EPS, None, ALU.add))
                dve.wait_ge(root_done, 1 if cols.start == 0 else 2)
                link(dve.reciprocal(bn_r[:, cols], bn_q[:, cols]))
                link(dve.tensor_tensor(bn_t[:, cols], bn_r[:, cols], bn_r[:, cols], ALU.mult))
                link(dve.scalar_tensor_tensor(bn_q[:, cols], bn_t[:, cols], -0.5, bn_v[:, cols], ALU.mult, ALU.mult))
                link(dve.scalar_tensor_tensor(bn_t[:, cols], bn_q[:, cols], 1.5, bn_r[:, cols], ALU.add, ALU.mult))
                link(dve.tensor_tensor(bn_s[:, cols], bn[:, 0, cols], bn_t[:, cols], ALU.mult))
                link(dve.tensor_tensor(bn_r[:, cols], bn[:, 2, cols], bn_s[:, cols], ALU.mult))
                link(dve.tensor_tensor(bn_b[:, cols], bn[:, 1, cols], bn_r[:, cols], ALU.subtract))

            dve.wait_ge(params_loaded, 16 * PARAMS)
            batch_norms(slice(0, 3))
            link(dve.tensor_scalar(w1bs[:], w1b, bn_s[:, 1:2], None, ALU.mult))
            link(dve.memset(wn[0:D, :], 0.0))
            link(dve.scalar_tensor_tensor(wn[D:P, :], w1c[D:P, :], bn_s[D:P, 2:3], w1bs[D:P, :], ALU.mult, ALU.add))
            link(dve.memset(w3_at[:], 0.0))
            for c in range(GC):
                for h in range(2):
                    link(dve.tensor_copy(w3_at[h * F2:(h + 1) * F2, c, 2 * c + h:2 * c + h + 1],
                                         w3[h * F2:(h + 1) * F2, :]))
            dve.wait_ge(bias_mm, 1)
            dve.tensor_tensor(c0[:], ps_m[:, 0:1], b1c[:], ALU.add).then_inc(weights_ready, 1)
            link(dve.scalar_tensor_tensor(wu[:], w1a, bn_s[:, 0:1], w1bs[:], ALU.mult, ALU.subtract))
            link(dve.tensor_copy(wu_h[:], wu[:]))
            link(dve.tensor_tensor(wu_l[:], wu[:], wu_h[:].bitcast(F32), ALU.subtract))
            dve.wait_ge(ident_set, 2)
            link(dve.tensor_copy(ident_r[:], ident[:]))
            dve.wait_ge(params2_loaded, 16 * PARAMS2)
            batch_norms(slice(3, 4))
            assert steps[0] == DIN_SHIFT
            link(dve.tensor_scalar(wd1s[:], wd1[:], bn_s[:, 3:4], None, ALU.mult))
            link(dve.memset(fw_col[:], 0.0))
            link(dve.tensor_copy(fw_col[:, 0:1], fw[:]))
            dve.wait_ge(bias_mm, 2)
            link(dve.tensor_tensor(bd1s[:], ps_m[0:NH, 1:3], bd1[:], ALU.add))
            dve.wait_ge(pre_mm, 3 * NB)
            dve.tensor_scalar(neg_c[:], neg_c[:], -1.0, None, ALU.mult).then_inc(negated, 1)
            dve.wait_ge(pre_mm, 3 * NB + 1)
            dve.tensor_scalar(neg_g[:], neg_g[:], -1.0, None, ALU.mult).then_inc(negated, 1)
            dve.memset(prod[:, 0, CW:], 0.0).then_inc(negated, 1)
            dve.wait_ge(negated, 3)

            def group(s, g):
                G = s * GROUPS + g
                for c in range(GC):
                    k = G * GC + c
                    if exists(k):
                        wait(dve, y_done, k - GC + 1)
                        for h in range(2):
                            dve.wait_ge(x_done, 2 * k + h + 1)
                            dve.tensor_tensor(h1[:, c, h * HC:(h + 1) * HC].rearrange("p (t b) -> p t b", b=P),
                                              ps_x[:, h * HC:(h + 1) * HC].rearrange("p (t b) -> p t b", b=P),
                                              neg_c[:, bass.ds(s * P, P)].unsqueeze(1).to_broadcast([P, HALF, P]),
                                              ALU.max).then_inc(h1_done, 1)
                    if exists(k - 1):
                        cb = (c - 1) % GC
                        s2, g2 = (s, g) if c >= 1 else back(s, g, 1)
                        dve.wait_ge(y_done, k)
                        wait(dve, z_done, k - GC)
                        dve.tensor_tensor(h2[:, cb * HC:(cb + 1) * HC].rearrange("p (t b) -> p t b", b=P),
                                          y_bank(cb).rearrange("p (t b) -> p t b", b=P),
                                          neg_g[:, bass.ds(s2 * P, P)].unsqueeze(1).to_broadcast([P, HALF, P]),
                                          ALU.max).then_inc(h2_done, 1)
                    if exists(k - 10):
                        cb = (c - 10) % GC
                        dve.wait_ge(prod_done, k - 9)
                        wait(dve, part_done, k - 10)
                        if c == GC - 1 and isinstance(g, int) and g == 1:
                            into = user[:, bass.ds(s - 1, 1), :].rearrange("p a d -> p (a d)")
                            dve.memset(prod[:, 0, CW:], 0.0)
                        else:
                            into = prod[:, (cb + 1) % GC, CW:]
                        red = dve.tensor_reduce(into, prod[:, cb, :].rearrange("p (t d) -> p d t", d=D), AX.X, ALU.add)
                        red.then_inc(part_done, 1)

            all_groups(dve, group)

            for step in range(NB + 1):
                if step < NB:
                    b = step
                    dve.wait_ge(d1_sum, 2 * (b + 1))
                    wait(dve, d2_mm, b - 1)
                    dve.scalar_tensor_tensor(d1v(b, 0), d1s(b, 0), NEG_SLOPE, d1s(b, 0), ALU.mult, ALU.max)
                    dve.scalar_tensor_tensor(d1v(b, 1), d1s(b, 1), NEG_SLOPE, d1s(b, 1), ALU.mult, ALU.max
                                             ).then_inc(d1_act, 1)
                if step >= 1:
                    b = step - 1
                    dve.wait_ge(d2_sum, b + 1)
                    dve.scalar_tensor_tensor(d2v(b), d2s(b), NEG_SLOPE, d2s(b), ALU.mult, ALU.max).then_inc(d2_act, 1)


_INS = ["r_inputs"] + ["L0_rec_" + n for n in (
    "att_bn_gamma", "att_bn_beta", "att_bn_mean", "att_bn_var",
    "att_W1", "att_b1", "att_W2", "att_b2", "att_W3", "att_b3",
    "din_bn_gamma", "din_bn_beta", "din_bn_mean", "din_bn_var",
    "din_W1", "din_b1", "din_W2", "din_b2", "f_W", "f_b")]


def kernel(**inputs):
    import numpy as _np
    import concourse.bacc as _bacc
    from concourse import mybir as _mybir
    from concourse.bass_utils import run_bass_kernel_spmd as _run

    nc = _bacc.Bacc("TRN2", target_bir_lowering=False, num_devices=1)
    arrays, args = {}, []
    for name in _INS:
        a = _np.ascontiguousarray(inputs[name])
        arrays[f"in_{name}"] = a
        args.append(nc.dram_tensor(f"in_{name}", a.shape, _mybir.dt.from_np(a.dtype), kind="ExternalInput").ap())
    users = inputs["r_inputs"].shape[0]
    args.append(nc.dram_tensor("out_0", (users, 1), _mybir.dt.float32, kind="ExternalOutput").ap())
    attention_head(nc, *args)
    r = _run(nc, [arrays], core_ids=[0])
    return r.results[0]["out_0"]
```
